# Optimizing a Trainium2 kernel written in Bass

```python
import numpy as np
import jax
import jax.numpy as jnp

def _softmax(x, axis=-1):
    return jax.nn.softmax(x, axis=axis)

def _gelu(x):
    return jax.nn.gelu(x, approximate=True)

def _silu(x):
    return jax.nn.silu(x)

def _sigmoid(x):
    return jax.nn.sigmoid(x)

def _layernorm(x, axis=-1, eps=1e-05):
    m = jnp.mean(x, axis=axis, keepdims=True)
    v = jnp.var(x, axis=axis, keepdims=True)
    return (x - m) / jnp.sqrt(v + eps)

def _scatter_add(tgt, idx, src, axis=0):
    return tgt.at[idx].add(src)

def _segment_sum(src, seg, n):
    return jax.ops.segment_sum(src, seg, n)
kernel_name = 'mk_vit_tower_cls_d1_tok_img256_r4_ca5121'

def setup_inputs(seed: int=0):
    np.random.seed(seed)
    _w = jnp.asarray

    def _rec_inputs():
        import jax
        import jax.numpy as jnp
        _rk = jax.random.key(seed)
        x = -0.000596345 + 1.00056 * jax.random.normal(jax.random.fold_in(_rk, 1), (128, 64, 64, 3), jnp.float32)
        cls_tok = 0.02 * jax.random.normal(jax.random.fold_in(_rk, 5), (1, 1, 64), jnp.float32)
        return (x, cls_tok)
    x, cls_tok = _rec_inputs()

    def _L0_tok_setup():
        import jax, jax.numpy as jnp
        import numpy as np
        M1 = 20
        M2 = 20

        def _spectral_conv(x, w):
            B, Cin, H, W = x.shape
            x_ft = jnp.fft.rfft2(x, norm='ortho')
            out = jnp.einsum('bixy,ioxy->boxy', x_ft[:, :, :M1, :M2], w.astype(x_ft.dtype))
            out_ft = jnp.zeros((B, w.shape[1], H, W // 2 + 1), dtype=x_ft.dtype)
            out_ft = out_ft.at[:, :, :M1, :M2].set(out)
            return jnp.fft.irfft2(out_ft, s=(H, W), norm='ortho')

        def _gelu(x):
            return jax.nn.gelu(x, approximate=False)
        key = jax.random.key(seed)
        ks = jax.random.split(key, 16)
        B, H, W, width = (16, 64, 64, 32)
        scale = 1.0 / (width * width)
        d = {}
        d['coords'] = jax.random.normal(ks[0], (B, H, W, 3), dtype=jnp.float32)
        d['fc0_w'] = jax.random.normal(ks[1], (3, width), dtype=jnp.float32) * 0.1
        d['fc0_b'] = jnp.zeros((width,), dtype=jnp.float32)
        for i in range(4):
            d[f'sw{i}'] = scale * jax.random.normal(ks[2 + i], (width, width, M1, M2), dtype=jnp.float32)
            d[f'cw{i}'] = jax.random.normal(ks[6 + i], (width, width), dtype=jnp.float32) * 0.1
            d[f'cb{i}'] = jnp.zeros((width,), dtype=jnp.float32)
        d['fc1_w'] = jax.random.normal(ks[10], (width, 64), dtype=jnp.float32) * 0.1
        d['fc1_b'] = jnp.zeros((64,), dtype=jnp.float32)
        d['fc2_w'] = jax.random.normal(ks[11], (64, 1), dtype=jnp.float32) * 0.1
        d['fc2_b'] = jnp.zeros((1,), dtype=jnp.float32)
        return d
    _L0_tok_all = _L0_tok_setup()
    _L0_tok_in = {k: v for k, v in _L0_tok_all.items() if k in ('fc0_w', 'fc0_b', 'sw0', 'cw0', 'cb0', 'sw1', 'cw1', 'cb1', 'sw2', 'cw2', 'cb2', 'sw3', 'cw3', 'cb3', 'fc1_w', 'fc1_b', 'fc2_w', 'fc2_b')}
    del _L0_tok_all

    def _L0_attn_setup():
        import jax, jax.numpy as jnp
        import numpy as np
        from functools import partial
        D_MODEL = 64
        D_INNER = 128
        D_STATE = 16
        DT_RANK = 16
        D_CONV = 4
        WS = 32
        LN_EPS = 1e-05

        def layernorm(x, g, b):
            mu = jnp.mean(x, axis=-1, keepdims=True)
            var = jnp.mean(jnp.square(x - mu), axis=-1, keepdims=True)
            return (x - mu) * jax.lax.rsqrt(var + LN_EPS) * g + b

        def silu(x):
            return x * jax.nn.sigmoid(x)

        def causal_depthwise_conv(x, w, b):
            lhs = jnp.swapaxes(x, 1, 2)
            rhs = w[:, None, :]
            out = jax.lax.conv_general_dilated(lhs, rhs, window_strides=(1,), padding=[(D_CONV - 1, 0)], dimension_numbers=('NCH', 'OIH', 'NCH'), feature_group_count=w.shape[0])
            out = out + b[None, :, None]
            return jnp.swapaxes(out, 1, 2)

        def selective_scan(u, delta, A, Bm, Cm, Dp):

            def step(h, inp):
                d_t, b_t, c_t, u_t = inp
                dA = jnp.exp(d_t[..., None] * A)
                h = dA * h + (d_t * u_t)[..., None] * b_t[:, None, :]
                y = jnp.einsum('bdn,bn->bd', h, c_t)
                return (h, y)
            N = u.shape[0]
            h0 = jnp.zeros((N, D_INNER, D_STATE), dtype=u.dtype)
            xs = (jnp.swapaxes(delta, 0, 1), jnp.swapaxes(Bm, 0, 1), jnp.swapaxes(Cm, 0, 1), jnp.swapaxes(u, 0, 1))
            _, ys = jax.lax.scan(step, h0, xs)
            return jnp.swapaxes(ys, 0, 1) + u * Dp

        def mamba_block(x, inproj_w, conv_w, conv_b, xproj_w, dtproj_w, dtproj_b, A_log, Dp, outproj_w):
            xz = jnp.einsum('nld,ed->nle', x, inproj_w)
            xm, z = jnp.split(xz, 2, axis=-1)
            xm = silu(causal_depthwise_conv(xm, conv_w, conv_b))
            xdbc = jnp.einsum('nld,ed->nle', xm, xproj_w)
            dt = xdbc[..., :DT_RANK]
            Bm = xdbc[..., DT_RANK:DT_RANK + D_STATE]
            Cm = xdbc[..., DT_RANK + D_STATE:]
            delta = jax.nn.softplus(jnp.einsum('nlr,dr->nld', dt, dtproj_w) + dtproj_b)
            A = -jnp.exp(A_log)
            y = selective_scan(xm, delta, A, Bm, Cm, Dp)
            y = y * silu(z)
            return jnp.einsum('nld,ed->nle', y, outproj_w)
        key = jax.random.key(seed)
        ks = jax.random.split(key, 20)
        f = jax.random.normal
        return {'x': f(ks[0], (8, 1024, D_MODEL), jnp.float32), 'in_w': f(ks[1], (D_MODEL, D_MODEL), jnp.float32) * 0.05, 'in_b': f(ks[2], (D_MODEL,), jnp.float32) * 0.05, 'ln_g': jnp.ones((D_MODEL,), jnp.float32), 'ln_b': jnp.zeros((D_MODEL,), jnp.float32), 'inproj_w': f(ks[3], (2 * D_INNER, D_MODEL), jnp.float32) * 0.05, 'conv_w': f(ks[4], (D_INNER, D_CONV), jnp.float32) * 0.2, 'conv_b': f(ks[5], (D_INNER,), jnp.float32) * 0.05, 'xproj_w': f(ks[6], (DT_RANK + 2 * D_STATE, D_INNER), jnp.float32) * 0.05, 'dtproj_w': f(ks[7], (D_INNER, DT_RANK), jnp.float32) * 0.1, 'dtproj_b': f(ks[8], (D_INNER,), jnp.float32) * 0.1, 'A_log': jax.random.uniform(ks[9], (D_INNER, D_STATE), jnp.float32), 'Dp': f(ks[10], (D_INNER,), jnp.float32) * 0.1, 'outproj_w': f(ks[11], (D_MODEL, D_INNER), jnp.float32) * 0.05, 'out_w': f(ks[12], (D_MODEL, D_MODEL), jnp.float32) * 0.05, 'out_b': f(ks[13], (D_MODEL,), jnp.float32) * 0.05, 'oln_g': jnp.ones((D_MODEL,), jnp.float32), 'oln_b': jnp.zeros((D_MODEL,), jnp.float32)}
    _L0_attn_all = _L0_attn_setup()
    _L0_attn_in = {k: v for k, v in _L0_attn_all.items() if k in ('in_w', 'in_b', 'ln_g', 'ln_b', 'inproj_w', 'conv_w', 'conv_b', 'xproj_w', 'dtproj_w', 'dtproj_b', 'A_log', 'Dp', 'outproj_w', 'out_w', 'out_b', 'oln_g', 'oln_b')}
    del _L0_attn_all

    def _L0_ffn_setup():
        import jax, jax.numpy as jnp
        import numpy as np
        B, S, H, F, E, K = (8, 1024, 64, 128, 16, 2)
        EPS = 1e-05
        key = jax.random.key(seed)
        ks = jax.random.split(key, 9)
        sc = 0.02
        return {'x': jax.random.normal(ks[0], (B, S, H), dtype=jnp.float32), 'gate_w': jax.random.normal(ks[1], (H, E), dtype=jnp.float32) * sc, 'gate_b': jnp.zeros((E,), dtype=jnp.float32), 'w1': jax.random.normal(ks[2], (E, H, F), dtype=jnp.float32) * sc, 'b1': jnp.zeros((E, F), dtype=jnp.float32), 'w2': jax.random.normal(ks[3], (E, F, H), dtype=jnp.float32) * sc, 'b2': jnp.zeros((E, H), dtype=jnp.float32), 'gamma': jnp.ones((H,), dtype=jnp.float32), 'beta': jnp.zeros((H,), dtype=jnp.float32)}
    _L0_ffn_all = _L0_ffn_setup()
    _L0_ffn_in = {k: v for k, v in _L0_ffn_all.items() if k in ('gate_w', 'gate_b', 'w1', 'b1', 'w2', 'b2', 'gamma', 'beta')}
    del _L0_ffn_all
    return {'x': x, 'cls_tok': cls_tok, 'L0_tok_fc0_w': _L0_tok_in['fc0_w'], 'L0_tok_fc0_b': _L0_tok_in['fc0_b'], 'L0_tok_sw0': _L0_tok_in['sw0'], 'L0_tok_cw0': _L0_tok_in['cw0'], 'L0_tok_cb0': _L0_tok_in['cb0'], 'L0_tok_sw1': _L0_tok_in['sw1'], 'L0_tok_cw1': _L0_tok_in['cw1'], 'L0_tok_cb1': _L0_tok_in['cb1'], 'L0_tok_sw2': _L0_tok_in['sw2'], 'L0_tok_cw2': _L0_tok_in['cw2'], 'L0_tok_cb2': _L0_tok_in['cb2'], 'L0_tok_sw3': _L0_tok_in['sw3'], 'L0_tok_cw3': _L0_tok_in['cw3'], 'L0_tok_cb3': _L0_tok_in['cb3'], 'L0_tok_fc1_w': _L0_tok_in['fc1_w'], 'L0_tok_fc1_b': _L0_tok_in['fc1_b'], 'L0_tok_fc2_w': _L0_tok_in['fc2_w'], 'L0_tok_fc2_b': _L0_tok_in['fc2_b'], 'L0_attn_in_w': _L0_attn_in['in_w'], 'L0_attn_in_b': _L0_attn_in['in_b'], 'L0_attn_ln_g': _L0_attn_in['ln_g'], 'L0_attn_ln_b': _L0_attn_in['ln_b'], 'L0_attn_inproj_w': _L0_attn_in['inproj_w'], 'L0_attn_conv_w': _L0_attn_in['conv_w'], 'L0_attn_conv_b': _L0_attn_in['conv_b'], 'L0_attn_xproj_w': _L0_attn_in['xproj_w'], 'L0_attn_dtproj_w': _L0_attn_in['dtproj_w'], 'L0_attn_dtproj_b': _L0_attn_in['dtproj_b'], 'L0_attn_A_log': _L0_attn_in['A_log'], 'L0_attn_Dp': _L0_attn_in['Dp'], 'L0_attn_outproj_w': _L0_attn_in['outproj_w'], 'L0_attn_out_w': _L0_attn_in['out_w'], 'L0_attn_out_b': _L0_attn_in['out_b'], 'L0_attn_oln_g': _L0_attn_in['oln_g'], 'L0_attn_oln_b': _L0_attn_in['oln_b'], 'L0_ffn_gate_w': _L0_ffn_in['gate_w'], 'L0_ffn_gate_b': _L0_ffn_in['gate_b'], 'L0_ffn_w1': _L0_ffn_in['w1'], 'L0_ffn_b1': _L0_ffn_in['b1'], 'L0_ffn_w2': _L0_ffn_in['w2'], 'L0_ffn_b2': _L0_ffn_in['b2'], 'L0_ffn_gamma': _L0_ffn_in['gamma'], 'L0_ffn_beta': _L0_ffn_in['beta']}

def reference(x, cls_tok, L0_tok_fc0_w, L0_tok_fc0_b, L0_tok_sw0, L0_tok_cw0, L0_tok_cb0, L0_tok_sw1, L0_tok_cw1, L0_tok_cb1, L0_tok_sw2, L0_tok_cw2, L0_tok_cb2, L0_tok_sw3, L0_tok_cw3, L0_tok_cb3, L0_tok_fc1_w, L0_tok_fc1_b, L0_tok_fc2_w, L0_tok_fc2_b, L0_attn_in_w, L0_attn_in_b, L0_attn_ln_g, L0_attn_ln_b, L0_attn_inproj_w, L0_attn_conv_w, L0_attn_conv_b, L0_attn_xproj_w, L0_attn_dtproj_w, L0_attn_dtproj_b, L0_attn_A_log, L0_attn_Dp, L0_attn_outproj_w, L0_attn_out_w, L0_attn_out_b, L0_attn_oln_g, L0_attn_oln_b, L0_ffn_gate_w, L0_ffn_gate_b, L0_ffn_w1, L0_ffn_b1, L0_ffn_w2, L0_ffn_b2, L0_ffn_gamma, L0_ffn_beta):
    import jax
    import jax.numpy as jnp

    def _L0_tok_ref(coords, fc0_w, fc0_b, sw0, cw0, cb0, sw1, cw1, cb1, sw2, cw2, cb2, sw3, cw3, cb3, fc1_w, fc1_b, fc2_w, fc2_b):
        import jax, jax.numpy as jnp
        import numpy as np
        M1 = 20
        M2 = 20

        def _spectral_conv(x, w):
            B, Cin, H, W = x.shape
            x_ft = jnp.fft.rfft2(x, norm='ortho')
            out = jnp.einsum('bixy,ioxy->boxy', x_ft[:, :, :M1, :M2], w.astype(x_ft.dtype))
            out_ft = jnp.zeros((B, w.shape[1], H, W // 2 + 1), dtype=x_ft.dtype)
            out_ft = out_ft.at[:, :, :M1, :M2].set(out)
            return jnp.fft.irfft2(out_ft, s=(H, W), norm='ortho')

        def _gelu(x):
            return jax.nn.gelu(x, approximate=False)
        x = coords @ fc0_w + fc0_b
        x = jnp.transpose(x, (0, 3, 1, 2))
        for sw, cw, cb in ((sw0, cw0, cb0), (sw1, cw1, cb1), (sw2, cw2, cb2), (sw3, cw3, cb3)):
            x1 = _spectral_conv(x, sw)
            x2 = jnp.einsum('bchw,oc->bohw', x, cw) + cb[None, :, None, None]
            x = _gelu(x1 + x2)
        x = jnp.transpose(x, (0, 2, 3, 1))
        x = _gelu(x @ fc1_w + fc1_b)
        return (x @ fc2_w + fc2_b)[..., 0]

    def _L0_attn_ref(x, in_w, in_b, ln_g, ln_b, inproj_w, conv_w, conv_b, xproj_w, dtproj_w, dtproj_b, A_log, Dp, outproj_w, out_w, out_b, oln_g, oln_b):
        import jax, jax.numpy as jnp
        import numpy as np
        from functools import partial
        D_MODEL = 64
        D_INNER = 128
        D_STATE = 16
        DT_RANK = 16
        D_CONV = 4
        WS = 32
        LN_EPS = 1e-05

        def layernorm(x, g, b):
            mu = jnp.mean(x, axis=-1, keepdims=True)
            var = jnp.mean(jnp.square(x - mu), axis=-1, keepdims=True)
            return (x - mu) * jax.lax.rsqrt(var + LN_EPS) * g + b

        def silu(x):
            return x * jax.nn.sigmoid(x)

        def causal_depthwise_conv(x, w, b):
            lhs = jnp.swapaxes(x, 1, 2)
            rhs = w[:, None, :]
            out = jax.lax.conv_general_dilated(lhs, rhs, window_strides=(1,), padding=[(D_CONV - 1, 0)], dimension_numbers=('NCH', 'OIH', 'NCH'), feature_group_count=w.shape[0])
            out = out + b[None, :, None]
            return jnp.swapaxes(out, 1, 2)

        def selective_scan(u, delta, A, Bm, Cm, Dp):

            def step(h, inp):
                d_t, b_t, c_t, u_t = inp
                dA = jnp.exp(d_t[..., None] * A)
                h = dA * h + (d_t * u_t)[..., None] * b_t[:, None, :]
                y = jnp.einsum('bdn,bn->bd', h, c_t)
                return (h, y)
            N = u.shape[0]
            h0 = jnp.zeros((N, D_INNER, D_STATE), dtype=u.dtype)
            xs = (jnp.swapaxes(delta, 0, 1), jnp.swapaxes(Bm, 0, 1), jnp.swapaxes(Cm, 0, 1), jnp.swapaxes(u, 0, 1))
            _, ys = jax.lax.scan(step, h0, xs)
            return jnp.swapaxes(ys, 0, 1) + u * Dp

        def mamba_block(x, inproj_w, conv_w, conv_b, xproj_w, dtproj_w, dtproj_b, A_log, Dp, outproj_w):
            xz = jnp.einsum('nld,ed->nle', x, inproj_w)
            xm, z = jnp.split(xz, 2, axis=-1)
            xm = silu(causal_depthwise_conv(xm, conv_w, conv_b))
            xdbc = jnp.einsum('nld,ed->nle', xm, xproj_w)
            dt = xdbc[..., :DT_RANK]
            Bm = xdbc[..., DT_RANK:DT_RANK + D_STATE]
            Cm = xdbc[..., DT_RANK + D_STATE:]
            delta = jax.nn.softplus(jnp.einsum('nlr,dr->nld', dt, dtproj_w) + dtproj_b)
            A = -jnp.exp(A_log)
            y = selective_scan(xm, delta, A, Bm, Cm, Dp)
            y = y * silu(z)
            return jnp.einsum('nld,ed->nle', y, outproj_w)
        B, T, D = x.shape
        h = jnp.einsum('btd,ed->bte', x, in_w) + in_b
        pad_len = (WS - T % WS) % WS
        if pad_len > 0:
            h = jnp.pad(h, ((0, 0), (0, pad_len), (0, 0)))
        T_pad = h.shape[1]
        nw = T_pad // WS
        h = h.reshape(B * nw, WS, D_MODEL)
        residual = h
        h = layernorm(h, ln_g, ln_b)
        h = mamba_block(h, inproj_w, conv_w, conv_b, xproj_w, dtproj_w, dtproj_b, A_log, Dp, outproj_w)
        h = h + residual
        h = h.reshape(B, T_pad, D_MODEL)[:, :T, :]
        out = jnp.einsum('btd,ed->bte', h, out_w) + out_b
        return layernorm(out, oln_g, oln_b)

    def _L0_ffn_ref(x, gate_w, gate_b, w1, b1, w2, b2, gamma, beta):
        import jax, jax.numpy as jnp
        import numpy as np
        B, S, H, F, E, K = (8, 1024, 64, 128, 16, 2)
        EPS = 1e-05
        gate_logits = x @ gate_w + gate_b
        topk_vals, topk_idx = jax.lax.top_k(gate_logits, K)
        topk_w = jax.nn.softmax(topk_vals, axis=-1)
        h = jax.nn.relu(jnp.einsum('bsh,ehf->bsef', x, w1) + b1)
        expert_out = jnp.einsum('bsef,efh->bseh', h, w2) + b2
        sel = jnp.take_along_axis(expert_out, topk_idx[:, :, :, None], axis=2)
        moe = jnp.sum(topk_w[..., None] * sel, axis=2)
        y = x + moe
        mu = jnp.mean(y, axis=-1, keepdims=True)
        var = jnp.var(y, axis=-1, keepdims=True)
        return (y - mu) / jnp.sqrt(var + EPS) * gamma + beta
    h = _L0_tok_ref(x, L0_tok_fc0_w, L0_tok_fc0_b, L0_tok_sw0, L0_tok_cw0, L0_tok_cb0, L0_tok_sw1, L0_tok_cw1, L0_tok_cb1, L0_tok_sw2, L0_tok_cw2, L0_tok_cb2, L0_tok_sw3, L0_tok_cw3, L0_tok_cb3, L0_tok_fc1_w, L0_tok_fc1_b, L0_tok_fc2_w, L0_tok_fc2_b)
    h = jnp.concatenate([jnp.broadcast_to(cls_tok, (h.shape[0], 1, h.shape[2])), h], axis=1)
    h = h + _L0_attn_ref(_layernorm(h, axis=-1), L0_attn_in_w, L0_attn_in_b, L0_attn_ln_g, L0_attn_ln_b, L0_attn_inproj_w, L0_attn_conv_w, L0_attn_conv_b, L0_attn_xproj_w, L0_attn_dtproj_w, L0_attn_dtproj_b, L0_attn_A_log, L0_attn_Dp, L0_attn_outproj_w, L0_attn_out_w, L0_attn_out_b, L0_attn_oln_g, L0_attn_oln_b)
    h = h + _L0_ffn_ref(_layernorm(h, axis=-1), L0_ffn_gate_w, L0_ffn_gate_b, L0_ffn_w1, L0_ffn_b1, L0_ffn_w2, L0_ffn_b2, L0_ffn_gamma, L0_ffn_beta)
    return h

_drawn_inputs = setup_inputs


def setup_inputs(seed=0):
    import zlib

    import numpy as np

    out = dict(_drawn_inputs(seed))
    spreads = {'L0_tok_fc0_b': (0.0, 0.519),
     'L0_tok_cb0': (0.0, 0.273),
     'L0_tok_cb1': (0.0, 0.1),
     'L0_tok_cb2': (0.0, 0.344),
     'L0_tok_cb3': (0.0, 0.1),
     'L0_tok_fc1_b': (0.0, 0.1),
     'L0_attn_ln_g': (1.0, 0.6),
     'L0_attn_ln_b': (0.0, 0.8),
     'L0_attn_oln_g': (1.0, 0.2),
     'L0_attn_oln_b': (0.0, 0.1),
     'L0_ffn_gate_b': (0.0, 0.1),
     'L0_ffn_b1': (0.0, 0.8),
     'L0_ffn_b2': (0.0, 0.271),
     'L0_ffn_gamma': (1.0, 0.2),
     'L0_ffn_beta': (0.0, 0.1)}
    factors = {'L0_tok_sw0': 8.0,
     'L0_tok_sw1': 8.0,
     'L0_tok_sw2': 8.0,
     'L0_tok_sw3': 8.0,
     'L0_attn_inproj_w': 6.09,
     'L0_attn_conv_w': 6.998,
     'L0_attn_conv_b': 8.0,
     'L0_attn_xproj_w': 8.0,
     'L0_attn_dtproj_w': 8.0,
     'L0_attn_dtproj_b': 8.0,
     'L0_attn_A_log': 8.0,
     'L0_attn_Dp': 42.824,
     'L0_attn_outproj_w': 6.053,
     'L0_ffn_w1': 5.906,
     'L0_ffn_w2': 5.397,
     'L0_attn_out_b': 8.0}
    for name, (base, spread) in spreads.items():
        noise = np.random.default_rng([zlib.crc32(name.encode()), seed]).standard_normal(out[name].shape)
        drawn = base * np.exp(spread * noise) if base else spread * noise
        out[name] = jnp.asarray(drawn.astype(out[name].dtype))
    for name, factor in factors.items():
        out[name] = (out[name] * factor).astype(out[name].dtype)
    return out
```

```python
import numpy as np
from contextlib import ExitStack

import concourse.bass as bass
from concourse import mybir

F32 = mybir.dt.float32
ACT = mybir.ActivationFunctionType
ALU = mybir.AluOpType
P = 128

B, H, W, CH, CIN = 128, 64, 64, 32, 3
M = 20
KR = 2 * M
CHUNK = 16
GI = 4
NG = CHUNK // GI
NCHUNK = B // CHUNK
LAYERS = 4
NB = 8
BC = 512
J = 4
KG = M // J
GX = NB * BC
DFT_N = 96
MIX_N = 96
MIX_K = 5
SK = M * 2 * CHUNK
FC1 = 64


def dft_constants():
    k, n = np.arange(M), np.arange(H)
    ang = 2 * np.pi * np.outer(n, k) / H
    cos, sin = np.cos(ang), np.sin(ang)
    fwd_w = np.zeros((P, DFT_N))
    fwd_re, fwd_im = np.zeros((P, DFT_N)), np.zeros((P, DFT_N))
    inv_h = np.zeros((P, P))
    inv_w = np.zeros((P, P))
    a = np.where(k == 0, 1.0, 2.0)
    for b in range(2):
        n0, k0 = 64 * b, KR * b
        fwd_w[n0:n0 + 64, k0:k0 + M] = cos / 8
        fwd_w[n0:n0 + 64, k0 + M:k0 + KR] = -sin / 8
        fwd_re[n0:n0 + 64, k0:k0 + KR:2] = cos / 8
        fwd_re[n0:n0 + 64, k0 + 1:k0 + KR:2] = -sin / 8
        fwd_im[n0:n0 + 64, k0:k0 + KR:2] = sin / 8
        fwd_im[n0:n0 + 64, k0 + 1:k0 + KR:2] = cos / 8
        inv_h[k0:k0 + KR:2, n0:n0 + 64] = cos.T / 8
        inv_h[k0 + 1:k0 + KR:2, n0:n0 + 64] = -sin.T / 8
        inv_w[k0:k0 + M, n0:n0 + 64] = (a * cos / 8).T
        inv_w[k0 + M:k0 + KR, n0:n0 + 64] = (-a * sin / 8).T
    return np.concatenate([fwd_w, fwd_re, fwd_im, inv_h, inv_w, np.eye(P)], 1).astype(np.float32)


def fno_program(nc, t, nchunk=NCHUNK):
    ctx = ExitStack()
    with ctx:
        def sb(name, shape):
            return ctx.enter_context(nc.sbuf_tensor(name, shape, F32))

        def sem(name):
            return ctx.enter_context(nc.semaphore(name))

        consts = sb("dft_consts", [P, 3 * DFT_N + 3 * P])
        fwd_w = consts[:, 0:DFT_N]
        fwd_h = [consts[:, DFT_N:2 * DFT_N], consts[:, 2 * DFT_N:3 * DFT_N]]
        inv_h = consts[:, 3 * DFT_N:3 * DFT_N + P]
        inv_w = consts[:, 3 * DFT_N + P:3 * DFT_N + 2 * P]
        ident = consts[:, 3 * DFT_N + 2 * P:3 * DFT_N + 3 * P]
        fc0_rhs = sb("fc0_rhs", [P, CH * 16])
        pw_rhs = sb("pw_rhs", [P, LAYERS, CH * J])
        dc_bias = sb("dc_bias", [CH, LAYERS, 2 * CHUNK])
        cb_raw = sb("cb_raw", [CH, LAYERS])
        fc1_lhs = sb("fc1_lhs", [P, 2, 2 * FC1])
        fc1_bias = sb("fc1_bias", [P, 1])
        fc2_rhs = sb("fc2_rhs", [P, 2])
        fc2_bias = sb("fc2_bias", [P, 1])
        coords = sb("coords", [P, 2, NB * P])
        mix_w = sb("mix_w", [P, KG * M, P])
        S = sb("S", [P, 2, KG, CHUNK, M, 2])
        D = sb("D", [P, 2 * 2 * M * CH])
        V = sb("V", [P, GX])
        x_T = sb("x_T", [P, NB, BC])
        x_X = sb("x_X", [P, NG, GX])
        Y = sb("Y", [P, 2 * KR, CH])
        y_flat = Y[:, :, :].rearrange("p k c -> p (k c)")
        g1 = y_flat[:, 0:2 * BC].rearrange("p (a n) -> p a n", a=2)
        rows_out = y_flat[:, 2 * BC:2 * BC + NG * P].rearrange("p (g n) -> p g n", g=NG)
        ev = [ctx.enter_context(nc.psum_tensor(f"ev{i}", [P, BC], F32)) for i in range(4)]
        ga = [ctx.enter_context(nc.psum_tensor(f"ga{i}", [P, BC], F32)) for i in range(3)]
        fc2_ps = ctx.enter_context(nc.psum_tensor("fc2_ps", [P, P], F32))
        N_EV, N_GA = len(ev), len(ga)

        cleared = sem("cleared")
        const_in = sem("const_in")
        bias_ready = sem("bias_ready")
        coords_in = [sem(f"coords_in{i}") for i in range(2)]
        mixw_in = sem("mixw_in")
        ev_ready = sem("ev_ready")
        ev_taken = sem("ev_taken")
        ga_ready = sem("ga_ready")
        ga_taken = sem("ga_taken")
        g1_used = sem("g1_used")
        rows_ready = sem("rows_ready")
        stored = sem("stored")

        TURN_D, INV_T, TURN_X, FWD_W, FWD_H, MIX_T = 5, 8, 8, 8, 2, KG * M // MIX_K
        TURN_V = TURN_S = TURN_X // 2
        EV_FIRST = NG * (TURN_V + FWD_W + FWD_H)
        EV_MID = MIX_T + NG * (TURN_D + INV_T + TURN_V + FWD_W + FWD_H)
        EV_LAST = MIX_T + NG * (TURN_D + INV_T + TURN_V)
        EV_CHUNK = EV_FIRST + (LAYERS - 1) * EV_MID + EV_LAST
        GA_MID = NG * (NB + TURN_S)
        G1_T = 16
        GA_LAST = NG * (NB + TURN_S + G1_T)
        GA_CHUNK = LAYERS * GA_MID + GA_LAST

        def phases(eng, run):
            def chunk_phases(chunk):
                ev_c, ga_c = chunk * EV_CHUNK, chunk * GA_CHUNK
                run("first", chunk, ev_c, ga_c, None)
                with eng.Fori(0, LAYERS - 1) as layer:
                    run("mid", chunk, ev_c + layer * EV_MID + EV_FIRST, ga_c + layer * GA_MID + GA_MID, layer)
                run("last", chunk, ev_c + (EV_FIRST + (LAYERS - 1) * EV_MID), ga_c + LAYERS * GA_MID, LAYERS - 1)
            with eng.Fori(0, nchunk) as chunk:
                chunk_phases(chunk)

        zeroed = [fc0_rhs[:, :], pw_rhs[:, :, :].rearrange("p a b -> p (a b)"),
                  fc1_lhs[:, :, :].rearrange("p a b -> p (a b)"), fc2_rhs[:, :],
                  mix_w[:, :, :].rearrange("p a b -> p (a b)"), D[:, :], V[:, :],
                  dc_bias[:, :, :].rearrange("p a b -> p (a b)")]

        block = ctx.enter_context(nc.Block())

        @block.gpsimd
        def _(pool):
            for tile in zeroed:
                pool.memset(tile, 0.0).then_inc(cleared, 1)
            pool.memset(coords[:, :, :].rearrange("p a b -> p (a b)"), 1.0).then_inc(cleared, 1)

        once = [(consts[:, :], t["dft"])]
        for h in range(16):
            once.append((fc0_rhs[3 * h:3 * h + 3, CH * h:CH * h + CH], t["fc0_w"]))
        once.append((fc0_rhs[48:49, :].rearrange("p (h c) -> p h c", c=CH),
                     t["fc0_b"].rearrange("(a x c) -> a x c", a=1, x=1).to_broadcast([1, 16, CH])))
        for l in range(LAYERS):
            for q in range(J):
                once.append((pw_rhs[CH * q:CH * q + CH, l, CH * q:CH * q + CH], t["cw"][l]))
            once.append((cb_raw[:, l:l + 1], t["cb"][l].rearrange("(c a) -> c a", a=1)))
        for half in range(2):
            for q in range(2):
                r = CH * (2 * half + q)
                once.append((fc1_lhs[r:r + CH, half, FC1 * q:FC1 * q + FC1], t["fc1_w"]))
        for q in range(2):
            once.append((fc1_bias[FC1 * q:FC1 * q + FC1, :], t["fc1_b"].rearrange("(f a) -> f a", a=1)))
            once.append((fc2_rhs[FC1 * q:FC1 * q + FC1, q:q + 1], t["fc2_w"]))
        once.append((fc2_bias[:, :], t["fc2_b"].rearrange("(a c) -> a c", a=1).to_broadcast([P, 1])))

        @block.sync
        def _(sp):
            sp.wait_ge(cleared, len(zeroed) + 1)
            sp.nop().then_inc(stored, 16)

            def load_coords(chunk, g):
                sp.dma_start(coords[0:48, g % 2, :], t["coords"][bass.ds(chunk * NG + g, 1), :, :]
                             .rearrange("a p n -> (a p) n")).then_inc(coords_in[g % 2], 16)

            def load_mix(l):
                for j in range(J):
                    sp.dma_start(mix_w[CH * j:CH * j + CH, :, CH * j:CH * j + CH], t["sw"][l * J + j])\
                        .then_inc(mixw_in, 16)

            for g in range(2):
                load_coords(0, g)
            with nc.allow_non_contiguous_dma(reason="small weights, once"):
                for dst, src in once:
                    sp.dma_start(dst, src).then_inc(const_in, 16)
            load_mix(0)

            def chunk_loads(chunk, more):
                for g in range(2, NG):
                    sp.wait_ge(ga_taken, chunk * GA_CHUNK + (g - 2) * (NB + TURN_S) + NB + 1)
                    load_coords(chunk, g)
                if more:
                    for g in range(2):
                        sp.wait_ge(ga_taken, chunk * GA_CHUNK + (g + 2) * (NB + TURN_S) + NB + 1)
                        load_coords(chunk + 1, g)
                for l in range(1, LAYERS):
                    sp.wait_ge(ev_taken, chunk * EV_CHUNK + EV_FIRST + (l - 1) * EV_MID + MIX_T + 1)
                    load_mix(l)
                if more:
                    sp.wait_ge(ev_taken, chunk * EV_CHUNK + EV_FIRST + (LAYERS - 1) * EV_MID + MIX_T + 1)
                    load_mix(0)
                for g in range(NG):
                    sp.wait_ge(rows_ready, chunk * NG + g + 2)
                    sp.dma_start(t["maps"][bass.ds(chunk * NG + g, 1), :, :].rearrange("a p n -> (a p) n"),
                                 rows_out[:, g, :]).then_inc(stored, 16)

            if nchunk > 1:
                with sp.Fori(0, nchunk - 1) as chunk:
                    chunk_loads(chunk, True)
            chunk_loads(nchunk - 1, False)
            sp.wait_ge(stored, 16 * nchunk * NG + 16)

        @block.tensor
        def _(pe):
            pe.nop().then_inc(g1_used, 1)
            pe.wait_ge(const_in, 16 * len(once))
            pe.wait_ge(bias_ready, 1)

            def run(kind, chunk, ev0, ga0, layer):
                n = {"ev": 0, "ga": 0}

                def ev_tile():
                    i = n["ev"]
                    pe.wait_ge(ev_taken, ev0 + max(i - N_EV + 1, 0) + 1)
                    n["ev"] += 1
                    return ev[i % N_EV]

                def ga_tile():
                    i = n["ga"]
                    pe.wait_ge(ga_taken, ga0 + max(i - N_GA + 1, 0) + 1)
                    n["ga"] += 1
                    return ga[i % N_GA]

                def mix():
                    if kind == "last":
                        pe.wait_ge(mixw_in, (chunk * LAYERS + LAYERS) * (16 * J))
                    else:
                        pe.wait_ge(mixw_in, (chunk * LAYERS + layer + 1) * (16 * J))
                    for i in range(MIX_T):
                        ps = ev_tile()
                        kg, k0 = i // (M // MIX_K), i % (M // MIX_K) * MIX_K
                        for k in range(MIX_K):
                            k1 = min(k0 + k, M - MIX_N // (2 * CHUNK))
                            out = ps[:, MIX_N * k:MIX_N * k + MIX_N]
                            dc = i == 0 and k == 0
                            last = pe.matmul(out, mix_w[:, kg * M + k0 + k, :],
                                             S[:, 0, kg, :, k1:k1 + MIX_N // (2 * CHUNK), :]
                                             .rearrange("p b k r -> p k b r"),
                                             start=True, stop=not dc)
                            if dc:
                                last = pe.matmul(out[:, 0:2 * CHUNK], ident[0:CH, :], dc_bias[:, bass.ds(layer, 1), :]
                                                 .rearrange("p a b -> p (a b)"), start=False, stop=True)
                        last.then_inc(ev_ready, 1)

                def turn_d(g):
                    for i in range(TURN_D):
                        ps = ev_tile()
                        for s in range(4):
                            u = 4 * i + s
                            b_hi, r, kg = u // (2 * KG), (u // KG) % 2, u % KG
                            b0 = g * GI + 2 * b_hi
                            rows = S[:, r, kg, b0:b0 + 2, :, :].rearrange("p b k r -> p (b k r)")
                            last = pe.transpose(ps[0:2 * KR, P * s:P * s + P], rows, ident)
                        last.then_inc(ev_ready, 1)

                def inverse_h(d_at):
                    pe.wait_ge(ev_taken, ev0 + d_at + 1)
                    for i in range(INV_T):
                        ps = ev_tile()
                        for s in range(4):
                            cols = D[:, :].rearrange("p (k c) -> p k c", c=CH)[:, :, 4 * i + s]
                            last = pe.matmul(ps[0:2 * KR, P * s:P * s + P], cols, inv_h, start=True, stop=True)
                        last.then_inc(ev_ready, 1)
                    return n["ev"]

                def project_coords(g):
                    pe.wait_ge(coords_in[g % 2], (chunk * (NG // 2) + g // 2 + 1) * 16)
                    for i in range(NB):
                        ps = ga_tile()
                        pe.matmul(ps[:, :], coords[:, g % 2, P * i:P * i + P], fc0_rhs[:, :],
                                  start=True, stop=True).then_inc(ga_ready, 1)

                def inverse_w_and_pointwise(g, v_at):
                    pe.wait_ge(ev_taken, ev0 + v_at + 1)
                    for i in range(NB):
                        ps = ga_tile()
                        v = V[:, :].rearrange("p (c n) -> p n c", c=CH)[:, 16 * i:16 * i + 16, :]
                        pe.matmul(ps[:, :], inv_w, v, start=True, stop=False)
                        for q in range(4):
                            col = (4 * i + q) * P
                            last = pe.matmul(ps[:, P * q:P * q + P], x_X[:, g, col:col + P],
                                             pw_rhs[:, bass.ds(layer, 1), :].rearrange("p a n -> p (a n)"),
                                             start=False, stop=q == 3)
                        last.then_inc(ga_ready, 1)

                def turn_x():
                    written = n["ga"] - NB
                    for i in range(TURN_X):
                        pe.wait_ge(ga_taken, ga0 + written + i + 2)
                        ps = ga_tile() if i % 2 else ev_tile()
                        for q in range(4):
                            last = pe.transpose(ps[:, P * q:P * q + P], x_T[:, i, P * q:P * q + P], ident)
                        last.then_inc(ga_ready if i % 2 else ev_ready, 1)
                    return n["ev"]

                def forward_w():
                    x_of = x_T[:, :, :].rearrange("p i (h c) -> p (i h) c", c=CH)
                    for i in range(FWD_W):
                        ps = ev_tile()
                        for s in range(4):
                            c = 4 * i + s
                            last = pe.matmul(ps[:, DFT_N * s:DFT_N * s + DFT_N],
                                             x_of[:, :, c], fwd_w, start=True, stop=True)
                        last.then_inc(ev_ready, 1)
                    return n["ev"]

                def forward_h(y_at):
                    pe.wait_ge(ev_taken, ev0 + y_at + 1)
                    for b_hi in range(FWD_H):
                        ps = ev_tile()
                        for kg in range(KG):
                            for r in range(2):
                                k0 = KR * b_hi + M * r + J * kg
                                last = pe.matmul(ps[:, DFT_N * kg:DFT_N * kg + DFT_N],
                                                 Y[:, k0:k0 + J, :].rearrange("p j c -> p (j c)"), fwd_h[r],
                                                 start=r == 0, stop=r == 1)
                        last.then_inc(ev_ready, 1)

                def head(g, x_at):
                    ga_base = n["ga"]

                    def fc2(m):
                        pe.wait_ge(ga_taken, ga0 + ga_base + m + 2)
                        if m == 0:
                            pe.wait_ge(rows_ready, chunk * NG + g + 1)
                        for q in range(4):
                            col = 16 * (m // 2) + 4 * q + 2 * (m % 2)
                            last = pe.matmul(fc2_ps[:, col:col + 2], g1[:, m % 2, P * q:P * q + P], fc2_rhs[:, :],
                                             start=True, stop=True)
                        last.then_inc(g1_used, 1)

                    for m in range(G1_T):
                        i, half = m // 2, m % 2
                        if half == 0 and i % 2 == 0:
                            pe.wait_ge(ev_taken, ev0 + x_at - TURN_V + i // 2 + 2)
                        if half == 0 and i % 2:
                            pe.wait_ge(ga_taken, ga0 + ga_base - TURN_S + i // 2 + 2)
                        ps = ga_tile()
                        pe.matmul(ps[:, :], fc1_lhs[:, half, :], x_X[:, g, BC * i:BC * i + BC],
                                  start=True, stop=True).then_inc(ga_ready, 1)
                        if m >= 1:
                            fc2(m - 1)
                    fc2(G1_T - 1)

                v_at = None
                if kind != "first":
                    mix()
                    pe.wait_ge(ev_taken, ev0 + MIX_T + 1)
                    turn_d(0)
                    v_at = inverse_h(n["ev"])
                for g in range(NG):
                    if kind == "first":
                        project_coords(g)
                    else:
                        inverse_w_and_pointwise(g, v_at)
                    x_at = turn_x()
                    if kind != "last":
                        y_at = forward_w()
                    more = kind != "first" and g + 1 < NG
                    if more:
                        turn_d(g + 1)
                        d_at = n["ev"]
                    if kind != "last":
                        forward_h(y_at)
                    if more:
                        v_at = inverse_h(d_at)
                    if kind == "last":
                        head(g, x_at)

            phases(pe, run)

        @block.vector
        def _(dve):
            dve.wait_ge(const_in, 16 * len(once))
            for l in range(LAYERS):
                last = dve.tensor_scalar(dc_bias[:, l, 0:2 * CHUNK:2], cb_raw[:, l:l + 1].to_broadcast([CH, CHUNK]),
                                         64.0, None, ALU.mult)
            last.then_inc(bias_ready, 1)
            dve.nop().then_inc(ev_taken, 1)
            dve.nop().then_inc(rows_ready, 1)

            def run(kind, chunk, ev0, ga0, layer):
                n = {"ev": 0}

                def ev_tile():
                    i = n["ev"]
                    dve.wait_ge(ev_ready, ev0 + i + 1)
                    n["ev"] += 1
                    return ev[i % N_EV]

                def take(dst, src):
                    dve.tensor_copy(dst, src).then_inc(ev_taken, 1)

                def mix():
                    for i in range(MIX_T):
                        ps = ev_tile()
                        kg, k0 = i // (M // MIX_K), i % (M // MIX_K) * MIX_K
                        z = ps[:, 0:MIX_K * MIX_N].rearrange("p (k n b r) -> p k n b r", k=MIX_K, r=2, b=CHUNK)
                        s = S[:, :, kg, :, k0:k0 + MIX_K, :].rearrange("p s b k r -> p s k b r")
                        own = [min(k0 + k, M - MIX_N // (2 * CHUNK)) for k in range(MIX_K)]
                        own = [k0 + k - own[k] for k in range(MIX_K)]
                        runs = [(0, MIX_K, 0)] if own[-1] == 0 else \
                            [(0, MIX_K - 2, 0), (MIX_K - 2, MIX_K - 1, 1), (MIX_K - 1, MIX_K, 2)]
                        for a, e, n_own in runs:
                            zz, ss = z[:, a:e, n_own], s[:, :, a:e]
                            dve.tensor_scalar(ss[:, 1, :, :, 1], zz[:, :, :, 0], -1.0, None, ALU.mult)
                            dve.tensor_copy(ss[:, 1, :, :, 0], zz[:, :, :, 1])
                            ins = dve.tensor_copy(ss[:, 0], zz)
                        ins.then_inc(ev_taken, 1)

                def turn_d():
                    for i in range(TURN_D):
                        take(D[0:2 * KR, BC * i:BC * i + BC], ev_tile()[0:2 * KR, :])

                def inverse_h():
                    for i in range(INV_T):
                        take(V[0:2 * KR, BC * i:BC * i + BC], ev_tile()[0:2 * KR, :])

                def turn_x(g):
                    for i in range(0, TURN_X, 2):
                        take(x_X[:, g, BC * i:BC * i + BC], ev_tile()[:, :])

                def forward_w():
                    for i in range(FWD_W):
                        ps = ev_tile()
                        take(Y[:, :, 4 * i:4 * i + 4],
                             ps[:, 0:4 * DFT_N].rearrange("p (c k) -> p k c", k=DFT_N)[:, 0:2 * KR, :])

                def forward_h(g):
                    for b_hi in range(FWD_H):
                        ps = ev_tile()
                        b0 = g * GI + 2 * b_hi
                        take(S[:, 0, :, b0:b0 + 2, :, :].rearrange("p g b k r -> p g (b k r)"),
                             ps[:, 0:KG * DFT_N].rearrange("p (g n) -> p g n", n=DFT_N)[:, :, 0:2 * KR])

                def maps(g):
                    dve.wait_ge(g1_used, chunk * (NG * G1_T) + G1_T * (g + 1) + 1)
                    dve.tensor_scalar(rows_out[:, g, :], fc2_ps[:, :], fc2_bias[:, :], None, ALU.add)\
                        .then_inc(rows_ready, 1)

                if kind != "first":
                    mix()
                    turn_d()
                    inverse_h()
                else:
                    dve.wait_ge(stored, chunk * (16 * NG) + 16)
                for g in range(NG):
                    turn_x(g)
                    if kind != "last":
                        forward_w()
                    more = kind != "first" and g + 1 < NG
                    if more:
                        turn_d()
                    if kind != "last":
                        forward_h(g)
                    if more:
                        inverse_h()
                    if kind == "last":
                        maps(g)

            phases(dve, run)

        @block.scalar
        def _(act):
            act.wait_ge(const_in, 16 * len(once))
            act.nop().then_inc(ga_taken, 1)

            def run(kind, chunk, ev0, ga0, layer):
                n = 0
                for g in range(NG):
                    for i in range(NB):
                        act.wait_ge(ga_ready, ga0 + n + 1)
                        act.activation(x_T[:, i, :], ga[n % N_GA][:, :], ACT.Copy if kind == "first" else ACT.Gelu)\
                            .then_inc(ga_taken, 1)
                        n += 1
                    for i in range(1, TURN_X, 2):
                        act.wait_ge(ga_ready, ga0 + n + 1)
                        act.activation(x_X[:, g, BC * i:BC * i + BC], ga[n % N_GA][:, :], ACT.Copy)\
                            .then_inc(ga_taken, 1)
                        n += 1
                    if kind == "last":
                        for m in range(G1_T):
                            act.wait_ge(ga_ready, ga0 + n + 1)
                            act.wait_ge(g1_used, chunk * (NG * G1_T) + max(G1_T * g + m - 1, 0) + 1)
                            act.activation(g1[:, m % 2, :], ga[n % N_GA][:, :], ACT.Gelu, bias=fc1_bias[:, :])\
                                .then_inc(ga_taken, 1)
                            n += 1

            phases(act, run)


DM, DI, DS, DTR, DC, WS = 64, 128, 16, 16, 4, 32
SEQ = H + 1
BLK = 2048
NBLK = B * H // BLK
TAIL = B
NTOK = B * SEQ
SUB = 1024
NE, FF = 16, 128
EPS = 1e-5
BF16 = mybir.dt.bfloat16
U32 = mybir.dt.uint32


def token_program(nc, t):
    ctx = ExitStack()
    with ctx:
        def sb(name, shape, dt=F32):
            return ctx.enter_context(nc.sbuf_tensor(name, shape, dt))

        padded = []

        def wide(name, cols):
            tile = sb(name, [P, cols])
            padded.append(tile[:, :])
            return tile, tile[0:DM, :]

        table = {}

        def sem(name, per_block=0):
            table[name] = (ctx.enter_context(nc.semaphore(name)), per_block)
            return name

        loads = []

        def load(name, shape, src):
            tile = sb(name, shape)
            loads.append((tile, src))
            return tile

        def load_wide(name, cols, src):
            tile, view = wide(name, cols)
            loads.append((view, src))
            return tile

        def column(name, n, src):
            return load(name, [n, 1], src.rearrange("(p a) -> p a", a=1))

        ident = load("t_ident", [P, P], t["dft"][:, 3 * DFT_N + 2 * P:3 * DFT_N + 3 * P])
        center = load_wide("center", DM, t["center"])
        average = load_wide("average", DM, t["average"])
        iota = load("iota", [P, NE], t["iota"])
        cls = load("cls", [DM, 1], t["cls"])
        in_w = load_wide("in_wt", DM, t["in_w"])
        in_b = column("in_b", DM, t["in_b"])
        ln_g, ln_b = column("ln_g", DM, t["ln_g"]), column("ln_b", DM, t["ln_b"])
        inproj = load_wide("inproj", 2 * DI, t["inproj"])
        conv_w = load("conv_w", [DI, DC], t["conv_w"])
        conv_b = column("conv_b", DI, t["conv_b"])
        xproj = load("xproj", [DI, DTR + 2 * DS], t["xproj"])
        dtproj = load("dtproj", [DTR, DI], t["dtproj"])
        dt_b = column("dt_b", DI, t["dt_b"])
        A = load("A", [DI, DS], t["A_log"])
        Dp = column("Dp", DI, t["Dp"])
        outproj = load("outproj", [DI, DM], t["outproj"])
        out_w = load_wide("out_wt", DM, t["out_w"])
        out_b = column("out_b", DM, t["out_b"])
        oln_g, oln_b = column("oln_g", DM, t["oln_g"]), column("oln_b", DM, t["oln_b"])
        gate_w = load_wide("gate_w", NE, t["gate_w"])
        gate_b = sb("gate_b", [P, NE])
        w1 = load_wide("w1", NE * FF, t["w1"].rearrange("d e f -> d (e f)"))
        b1 = load("b1", [FF, NE], t["b1"])
        w2 = load("w2", [FF, NE, DM], t["w2"])
        b2 = load("b2", [NE, DM], t["b2"])
        gamma, beta = column("gamma", DM, t["gamma"]), column("beta", DM, t["beta"])
        eps = sb("eps", [P, 1])
        sel = sb("sel", [P, 32, P], BF16)

        raw = sb("raw", [DM, BLK])
        h0_all, h0 = wide("h0", BLK)
        last_tok = sb("last_tok", [DM, B])
        (sq_all, sq), (nrm_all, nrm) = wide("sq", BLK), wide("nrm", BLK)
        std = sb("std", [DM, BLK])
        res_all, res = wide("res", BLK)
        conv = sb("conv", [DI, BLK])
        u, sz = sb("u", [DI, BLK]), sb("sz", [DI, BLK])
        dt_s = sb("dt_s", [DTR, BLK])
        parts = sb("parts", [P, BLK], BF16)
        part2 = sb("part2", [32, BLK], BF16)
        rest = sb("rest", [32, BLK])
        delta, du = sb("delta", [DI, BLK]), sb("du", [DI, BLK])
        decay = [sb(f"decay{i}", [DI, SUB]) for i in range(2)]
        dbu, hs = sb("dbu", [DI, SUB]), sb("hs", [DI, SUB])
        hc = [sb(f"hc{i}", [DI, SUB]) for i in range(2)]
        yz = sb("yz", [DI, BLK])
        (h1_all, h1), (xn_all, xn) = wide("h1", BLK), wide("xn", BLK)
        logits = sb("logits", [P, BLK // P, NE])
        top_v = sb("top_v", [P, BLK // P, 8])
        top_i = sb("top_i", [P, BLK // P, 8], U32)
        top_f = sb("top_f", [P, BLK // P, 2])
        gw = sb("gw", [P, 3, BLK // P])
        gate = sb("gate", [P, BLK // P, NE])
        gate2 = sb("gate2", [P, BLK // P, NE])
        gate_t = sb("gate_t", [NE, BLK])
        hid = [sb(f"hid{i}", [FF, BC]) for i in range(2)]
        hid_g = [sb(f"hid_g{i}", [FF, BC]) for i in range(2)]
        psA = ctx.enter_context(nc.psum_tensor("psA", [P, BLK], F32))
        psB = ctx.enter_context(nc.psum_tensor("psB", [P, BLK], F32))

        N_ZERO = 5 + len(padded)
        NSUB = BLK // SUB
        NS_ALL = NSUB * DS
        NTL = BLK // BC
        weights_in, zeroed = sem("weights_in"), sem("zeroed")
        consts_ready = sem("consts_ready")
        maps_in = sem("maps_in", 2)
        raw_free = sem("raw_free", 1)
        h0_ready = sem("h0_ready", 1)
        centered = sem("centered", 5)
        squared = sem("squared", 5)
        variance = sem("variance", 5)
        std_ready = sem("std_ready", 5)
        normed = sem("normed", 4)
        hin_ready = sem("hin_ready", 1)
        res_ready = sem("res_ready", 1)
        xz_ready = sem("xz_ready", 1)
        conv_ready = sem("conv_ready", 1)
        u_ready = sem("u_ready", 1)
        dtbc_ready = sem("dtbc_ready", 1)
        dt_ready = sem("dt_ready", 1)
        parts_ready = sem("parts_ready", 2)
        draw_ready = sem("draw_ready", 1)
        soft_ready = sem("soft_ready", 3)
        delta_ready = sem("delta_ready", 1)
        bc_ready = sem("bc_ready", 2 * NS_ALL)
        b_used = sem("b_used", NS_ALL)
        decay_ready = sem("decay_ready", NS_ALL)
        scanned = sem("scanned", NS_ALL)
        hc_ready = sem("hc_ready", NS_ALL)
        y_added = sem("y_added", NS_ALL)
        yz_ready = sem("yz_ready", NSUB)
        proj_ready = sem("proj_ready", 2)
        hr_ready = sem("hr_ready", 3)
        gl_ready = sem("gl_ready", 1)
        top_ready = sem("top_ready", 1)
        ge_ready = sem("ge_ready", 1)
        gate_ready = sem("gate_ready", 1)
        gateT_ready = sem("gateT_ready", 1)
        hid_ready = sem("hid_ready", NTL * NE)
        relu_ready = sem("relu_ready", NTL * NE)
        gated = sem("gated", NTL * NE)
        hid_used = sem("hid_used", NTL * NE)
        out_ready = sem("out_ready", 1)
        stored = sem("tok_stored", 1)
        chain = sem("chain")
        CHAIN = 34
        wait_passed = sem("wait_passed")
        consts_ready2 = sem("a_ready")

        block = ctx.enter_context(nc.Block())

        def blocks(eng, body):
            with eng.Fori(0, NBLK) as blk:
                body(blk, BLK, WS)
            body(NBLK, TAIL, 1)

        def stand_alone(eng):
            eng.nop().then_inc(S_(wait_passed), 1)

        def counters(eng, blk, alone=False):
            seen, before = {}, {}

            def base(per):
                if per not in before:
                    before[per] = blk * per if isinstance(blk, int) else eng.snap(blk * per)
                return before[per]

            def wait(name, k=None, unit=1):
                s, per = table[name]
                k = seen.get(name, 0) + 1 if k is None else k
                seen[name] = k
                eng.wait_ge(s, base(per * unit) + k * unit)
                if alone:
                    stand_alone(eng)
            wait.base = base
            return wait

        def S_(name):
            return table[name][0]

        def cut(w):
            return [(c, min(BC, w - c)) for c in range(0, w, BC)]

        def tile_loop(eng, blk, w, body):
            if w == BLK:
                with eng.Fori(0, NTL) as i:
                    body(i * BC, BC, eng.snap(blk * (NTL * NE) + i * NE))
            else:
                body(0, w, blk * NTL * NE)

        @block.gpsimd
        def _(pool):
            pool.nop().then_inc(S_(raw_free), 1)
            pool.memset(eps[:, :], EPS).then_inc(S_(zeroed), 1)
            for d in decay:
                pool.memset(d[:, :], 0.0).then_inc(S_(zeroed), 1)
            pool.memset(parts[:, :], 0.0).then_inc(S_(zeroed), 1)
            for tile in padded:
                pool.memset(tile, 0.0).then_inc(S_(zeroed), 1)
            pool.memset(sel[:, :, :].rearrange("p a b -> p (a b)"), 0.0).then_inc(S_(zeroed), 1)
            pool.wait_ge(S_(weights_in), 16 * (len(loads) + 1))

            def body(blk, w, win):
                wait = counters(pool, blk, True)
                wait(maps_in, 2, 16) if w == BLK else None
                if w == BLK:
                    pool.wait_ge(S_(out_ready), blk + 1)
                    stand_alone(pool)
                    n = B // NBLK
                    v = h0[:, :].rearrange("p (b t) -> p b t", t=H)
                    r = raw[:, :].rearrange("p (b t) -> p b t", t=H)
                    pool.tensor_copy(v[:, :, 1:H], r[:, :, 0:H - 1])
                    pool.tensor_copy(v[:, :, 0:1], cls[:, :].rearrange("p (a b) -> p a b", a=1).to_broadcast([DM, n, 1]))
                    pool.tensor_copy(last_tok[:, bass.ds(blk * n, n)].rearrange("p (b a) -> p b a", a=1), r[:, :, H - 1:H])\
                        .then_inc(S_(h0_ready), 1)
                    stand_alone(pool)
                    pool.wait_ge(S_(h0_ready), blk + 1)
                    stand_alone(pool)
                    pool.nop().then_inc(S_(raw_free), 1)
                else:
                    pool.wait_ge(S_(out_ready), blk + 1)
                    pool.wait_ge(S_(h0_ready), NBLK)
                    pool.tensor_copy(h0[:, 0:TAIL], last_tok[:, :]).then_inc(S_(h0_ready), 1)
            blocks(pool, body)

        @block.sync
        def _(sp):
            sp.wait_ge(S_(zeroed), N_ZERO)
            with nc.allow_non_contiguous_dma(reason="small weights, once"):
                for dst, src in loads:
                    sp.dma_start(dst[tuple(slice(None) for _ in dst.shape)], src).then_inc(S_(weights_in), 16)
                sp.dma_start(gate_b[:, :], t["gate_b"].rearrange("(a e) -> a e", a=1).to_broadcast([P, NE]))\
                    .then_inc(S_(weights_in), 16)
            sp.nop().then_inc(S_(stored), 16)
            gpb = B // GI // NBLK

            def body(blk, w, win):
                if w == BLK:
                    sp.wait_ge(S_(raw_free), blk + 1)
                    for b_hi in range(2):
                        dst = raw[:, :].rearrange("p (g a n) -> p g a n", g=gpb, a=2)[:, :, b_hi, :]
                        src = t["maps"][bass.ds(blk * gpb, gpb), W * b_hi:W * b_hi + W, :].rearrange("g p n -> p g n")
                        sp.dma_start(dst, src).then_inc(S_(maps_in), 16)
                sp.wait_ge(S_(out_ready), blk + 2)
                sp.dma_start(t["out"][:, bass.ds(blk * BLK, w)], nrm[:, 0:w]).then_inc(S_(stored), 16)
            blocks(sp, body)
            sp.wait_ge(S_(stored), 16 * (NBLK + 2))

        @block.tensor
        def _(pe):
            pe.wait_ge(S_(weights_in), 16 * (len(loads) + 1))
            pe.wait_ge(S_(consts_ready), 1)
            pe.nop().then_inc(S_(hid_used), 1)

            def body(blk, w, win):
                wait = counters(pe, blk)

                def product(ps, rows, lhs, rhs, start=True, stop=True):
                    for c, n in cut(w):
                        last = pe.matmul(ps[0:rows, c:c + n], lhs, rhs[:, c:c + n], start=start, stop=stop)
                    return last

                def layernorm(src):
                    product(psA, DM, center[:, :], src).then_inc(S_(centered), 1)
                    wait(squared)
                    product(psB, DM, average[:, :], sq_all).then_inc(S_(variance), 1)

                wait(h0_ready)
                layernorm(h0_all)
                wait(normed)
                product(psB, DM, in_w[:, :], nrm_all).then_inc(S_(hin_ready), 1)
                wait(res_ready)
                layernorm(res_all)
                wait(normed)
                product(psA, DI, inproj[:, 0:DI], nrm_all)
                product(psB, DI, inproj[:, DI:2 * DI], nrm_all).then_inc(S_(xz_ready), 1)
                wait(u_ready)
                product(psA, DTR, xproj[:, 0:DTR], u)
                product(psB, 2 * DS, xproj[:, DTR:DTR + 2 * DS], u).then_inc(S_(dtbc_ready), 1)
                wait(dt_ready)
                product(psA, DI, dtproj[:, :], dt_s).then_inc(S_(draw_ready), 1)
                wait(parts_ready)
                wait(soft_ready, 1)
                ws = min(SUB, w)
                slots = [psA[:, SUB:2 * SUB], psB[:, 0:SUB], psB[:, SUB:2 * SUB]]
                subs = max(w // SUB, 1)
                for s in range(subs):
                    c0 = s * SUB

                    def broadcast(n, which):
                        i = 2 * (DS * s + n) + which
                        if i >= 3:
                            wait(hc_ready if (i - 3) % 2 else b_used, (i - 3) // 2 + 1)
                        for c, m in cut(ws):
                            last = pe.matmul(slots[i % 3][:, c:c + m], sel[:, n + DS * which, :],
                                             parts[:, c0 + c:c0 + c + m], start=True, stop=True)
                        last.then_inc(S_(bc_ready), 1)

                    def add_y(n):
                        wait(hc_ready, DS * s + n + 1)
                        if s and n == 0:
                            wait(yz_ready, s)
                        for c, m in cut(ws):
                            last = pe.matmul(psA[:, c:c + m], ident[:, :], hc[n % 2][:, c:c + m],
                                             start=n == 0, stop=n == DS - 1)
                        last.then_inc(S_(y_added), 1)

                    for n in range(DS):
                        broadcast(n, 0)
                        broadcast(n, 1)
                        if n:
                            add_y(n - 1)
                    add_y(DS - 1)
                wait(yz_ready, subs)
                product(psA, DM, outproj[:, :], yz).then_inc(S_(proj_ready), 1)
                wait(hr_ready)
                product(psB, DM, out_w[:, :], xn_all).then_inc(S_(proj_ready), 1)
                wait(hr_ready)
                layernorm(xn_all)
                wait(normed)
                layernorm(h1_all)
                wait(normed)
                for i in range(w // P):
                    last = pe.matmul(psA[:, NE * i:NE * i + NE], xn_all[:, P * i:P * i + P], gate_w[:, :],
                                     start=True, stop=True)
                last.then_inc(S_(gl_ready), 1)
                wait(gate_ready)
                for i in range(w // P):
                    last = pe.transpose(psB[0:NE, P * i:P * i + P], gate[:, i, :], ident[:, :])
                last.then_inc(S_(gateT_ready), 1)
                wait(parts_ready)
                product(psA, DM, b2[:, :], gate_t, stop=False)

                def experts(c, m, done):
                    def second(e):
                        pe.wait_ge(S_(gated), done + e + 2)
                        stand_alone(pe)
                        pe.matmul(psA[0:DM, bass.ds(c, m)], w2[:, e, :], hid_g[e % 2][:, 0:m],
                                  start=False, stop=e == NE - 1).then_inc(S_(hid_used), 1)

                    for e in range(NE):
                        pe.wait_ge(S_(gated), done + max(e - 1, 0) + 1)
                        stand_alone(pe)
                        k = e % 2
                        pe.matmul(psB[:, BC * k:BC * k + m], w1[:, FF * e:FF * e + FF], xn_all[:, bass.ds(c, m)], start=True, stop=True)
                        pe.matmul(psB[:, BC * (2 + k):BC * (2 + k) + m], sel[:, e, :], parts[:, bass.ds(c, m)],
                                  start=True, stop=True).then_inc(S_(hid_ready), 1)
                        if e:
                            second(e - 1)
                    second(NE - 1)

                tile_loop(pe, blk, w, experts)
                wait(hr_ready)
                layernorm(res_all)

            blocks(pe, body)

        @block.scalar
        def _(act):
            act.wait_ge(S_(weights_in), 16 * (len(loads) + 1))
            act.wait_ge(S_(zeroed), N_ZERO)
            act.activation(A[:, :], A[:, :], ACT.Exp).then_inc(S_(consts_ready2), 1)
            act.wait_ge(S_(consts_ready), 1)

            def body(blk, w, win):
                wait = counters(act, blk)

                def layernorm():
                    wait(centered)
                    act.activation(sq[:, 0:w], psA[0:DM, 0:w], ACT.Square).then_inc(S_(squared), 1)
                    wait(variance)
                    act.activation(std[:, 0:w], psB[0:DM, 0:w], ACT.Sqrt, bias=eps[0:DM, :]).then_inc(S_(std_ready), 1)

                layernorm()
                layernorm()
                wait(xz_ready)
                act.activation(sz[:, 0:w], psB[:, 0:w], ACT.Silu)
                wait(conv_ready)
                act.activation(u[:, 0:w], conv[:, 0:w], ACT.Silu, bias=conv_b[:, :]).then_inc(S_(u_ready), 1)
                wait(dtbc_ready)
                act.activation(dt_s[:, 0:w], psA[0:DTR, 0:w], ACT.Copy).then_inc(S_(dt_ready), 1)
                wait(draw_ready)
                act.activation(du[:, 0:w], psA[:, 0:w], ACT.Relu, bias=dt_b[:, :])
                act.activation(delta[:, 0:w], psA[:, 0:w], ACT.Abs, bias=dt_b[:, :]).then_inc(S_(soft_ready), 1)
                wait(soft_ready, 1)
                act.activation(delta[:, 0:w], delta[:, 0:w], ACT.Exp, scale=-1.0).then_inc(S_(soft_ready), 1)
                wait(soft_ready, 2)
                act.activation(delta[:, 0:w], delta[:, 0:w], ACT.Ln, bias=1.0).then_inc(S_(soft_ready), 1)
                wait(delta_ready)
                if win > 1:
                    for i in range(NSUB * DS):
                        s, n = i // DS, i % DS
                        if i >= 2:
                            wait(scanned, i - 1)
                        d = decay[i % 2][:, :].rearrange("p (a b) -> p a b", b=WS)[:, :, 1:WS]
                        src = delta[:, SUB * s:SUB * s + SUB].rearrange("p (a b) -> p a b", b=WS)[:, :, 1:WS]
                        act.activation(d, src, ACT.Exp, scale=A[:, n:n + 1]).then_inc(S_(decay_ready), 1)
                layernorm()
                layernorm()
                wait(top_ready)
                n = w // P
                act.activation(gw[:, 0, 0:n], gw[:, 0, 0:n], ACT.Exp).then_inc(S_(ge_ready), 1)

                def experts(c, m, done):
                    for e in range(NE):
                        act.wait_ge(S_(hid_ready), done + e + 1)
                        act.wait_ge(S_(gated), done + max(e - 1, 0) + 1)
                        act.activation(hid[e % 2][:, 0:m], psB[:, BC * (e % 2):BC * (e % 2) + m], ACT.Relu,
                                       bias=b1[:, e:e + 1]).then_inc(S_(relu_ready), 1)

                tile_loop(act, blk, w, experts)
                layernorm()

            blocks(act, body)

        @block.vector
        def _(dve):
            links = [0]

            dve.wait_ge(S_(weights_in), 16 * (len(loads) + 1))
            dve.wait_ge(S_(zeroed), N_ZERO)
            for q in range(3):
                r = slice(32 * q, 32 * q + 32)
                dve.tensor_copy(sel[r, :, :], ident[r, r].rearrange("p (n a) -> p n a", a=1).to_broadcast([32, 32, P]))
            dve.wait_ge(S_(consts_ready2), 1)
            dve.tensor_scalar(A[:, :], A[:, :], -1.0, None, ALU.mult).then_inc(S_(consts_ready), 1)
            dve.nop().then_inc(S_(out_ready), 1)
            dve.nop().then_inc(S_(gated), 1)

            def body(blk, w, win):
                wait = counters(dve, blk)
                n_link = [0]

                def link(ins):
                    n_link[0] += 1
                    ins.then_inc(S_(chain), 1)
                    dve.wait_ge(S_(chain), wait.base(CHAIN) + n_link[0])

                def layernorm(dst, g=None, b=None, add=None):
                    wait(std_ready)
                    link(dve.reciprocal(std[:, 0:w], std[:, 0:w]))
                    ins = dve.tensor_tensor(dst[:, 0:w], psA[0:DM, 0:w], std[:, 0:w], ALU.mult)
                    if g is not None:
                        link(ins)
                        ins = dve.tensor_scalar(dst[:, 0:w], dst[:, 0:w], g[:, :], b[:, :], ALU.mult, ALU.add)
                    if add is not None:
                        link(ins)
                        ins = dve.tensor_tensor(dst[:, 0:w], dst[:, 0:w], add[:, 0:w], ALU.add)
                    return ins

                def split(src, rows):
                    link(dve.tensor_copy(parts[0:rows, 0:w], src))
                    link(dve.tensor_tensor(rest[0:rows, 0:w], src, parts[0:rows, 0:w], ALU.subtract))
                    link(dve.tensor_copy(part2[0:rows, 0:w], rest[0:rows, 0:w]))
                    dve.tensor_copy(parts[32:32 + rows, 0:w], part2[0:rows, 0:w])
                    dve.tensor_tensor(parts[64:64 + rows, 0:w], rest[0:rows, 0:w], part2[0:rows, 0:w], ALU.subtract)\
                        .then_inc(S_(parts_ready), 1)

                dve.wait_ge(S_(stored), blk * 16 + 16)
                layernorm(nrm).then_inc(S_(normed), 1)
                wait(hin_ready)
                dve.tensor_scalar(res[:, 0:w], psB[0:DM, 0:w], in_b[:, :], None, ALU.add).then_inc(S_(res_ready), 1)
                layernorm(nrm, ln_g, ln_b).then_inc(S_(normed), 1)
                wait(xz_ready)
                ins = dve.tensor_scalar(conv[:, 0:w], psA[:, 0:w], conv_w[:, DC - 1:DC], None, ALU.mult)
                if win > 1:
                    for s in range(1, DC):
                        link(ins)
                        o = conv[:, 0:w].rearrange("p (a b) -> p a b", b=WS)
                        x = psA[:, 0:w].rearrange("p (a b) -> p a b", b=WS)
                        ins = dve.scalar_tensor_tensor(out=o[:, :, s:WS], in0=x[:, :, 0:WS - s],
                                                       scalar=conv_w[:, DC - 1 - s:DC - s], in1=o[:, :, s:WS],
                                                       op0=ALU.mult, op1=ALU.add)
                ins.then_inc(S_(conv_ready), 1)
                wait(dtbc_ready)
                split(psB[0:2 * DS, 0:w], 2 * DS)
                wait(soft_ready, 3)
                link(dve.tensor_tensor(delta[:, 0:w], delta[:, 0:w], du[:, 0:w], ALU.add))
                dve.tensor_tensor(du[:, 0:w], delta[:, 0:w], u[:, 0:w], ALU.mult).then_inc(S_(delta_ready), 1)
                wait(delta_ready)
                ws = min(SUB, w)
                slots = [psA[:, SUB:2 * SUB], psB[:, 0:SUB], psB[:, SUB:2 * SUB]]
                for s in range(max(w // SUB, 1)):
                    cols = slice(s * SUB, s * SUB + ws)
                    for n in range(DS):
                        i = DS * s + n
                        wait(bc_ready, 2 * i + 1)
                        if win == 1 and i:
                            wait(hc_ready, i)
                        dve.tensor_tensor(dbu[:, 0:ws], slots[2 * i % 3][:, 0:ws], du[:, cols], ALU.mult)\
                            .then_inc(S_(b_used), 1)
                        wait(b_used, i + 1)
                        state = dbu
                        if win > 1:
                            wait(decay_ready, i + 1)
                            dve.tensor_tensor_scan(hs[:, :], decay[i % 2][:, :], dbu[:, :], 0.0, ALU.mult, ALU.add)\
                                .then_inc(S_(scanned), 1)
                            wait(scanned, i + 1)
                            state = hs
                        wait(bc_ready, 2 * i + 2)
                        if i >= 2:
                            wait(y_added, i - 1)
                        dve.tensor_tensor(hc[i % 2][:, 0:ws], state[:, 0:ws], slots[(2 * i + 1) % 3][:, 0:ws], ALU.mult)\
                            .then_inc(S_(hc_ready), 1)
                    wait(y_added, DS * (s + 1))
                    link(dve.scalar_tensor_tensor(out=yz[:, cols], in0=u[:, cols], scalar=Dp[:, :], in1=psA[:, 0:ws],
                                                  op0=ALU.mult, op1=ALU.add))
                    dve.tensor_tensor(yz[:, cols], yz[:, cols], sz[:, cols], ALU.mult).then_inc(S_(yz_ready), 1)
                wait(proj_ready, 1)
                dve.tensor_tensor(xn[:, 0:w], psA[0:DM, 0:w], res[:, 0:w], ALU.add).then_inc(S_(hr_ready), 1)
                wait(proj_ready, 2)
                dve.tensor_scalar(xn[:, 0:w], psB[0:DM, 0:w], out_b[:, :], None, ALU.add).then_inc(S_(hr_ready), 1)
                layernorm(h1, oln_g, oln_b, h0).then_inc(S_(normed), 1)
                layernorm(xn).then_inc(S_(normed), 1)

                n = w // P
                wait(gl_ready)
                link(dve.tensor_tensor(logits[:, 0:n, :], psA[:, 0:NE * n].rearrange("p (i e) -> p i e", e=NE),
                                       gate_b[:, :].rearrange("p (a e) -> p a e", a=1).to_broadcast([P, n, NE]), ALU.add))
                stand_alone(dve)
                for i in range(n):
                    ins = dve.max(top_v[:, i, :], logits[:, i, :])
                link(ins)
                dve.tensor_tensor(gw[:, 0, 0:n], top_v[:, 0:n, 1], top_v[:, 0:n, 0], ALU.subtract)\
                    .then_inc(S_(top_ready), 1)
                for i in range(n):
                    ins = dve.max_index(top_i[:, i, :], top_v[:, i, :], logits[:, i, :])
                link(ins)
                link(dve.tensor_copy(top_f[:, 0:n, :], top_i[:, 0:n, 0:2]))
                wait(ge_ready)
                link(dve.tensor_scalar(gw[:, 1, 0:n], gw[:, 0, 0:n], 1.0, None, ALU.add))
                link(dve.reciprocal(gw[:, 1, 0:n], gw[:, 1, 0:n]))
                link(dve.tensor_tensor(gw[:, 2, 0:n], gw[:, 0, 0:n], gw[:, 1, 0:n], ALU.mult))
                for k, g in enumerate((gate, gate2)):
                    at = [P, n, NE]
                    link(dve.tensor_tensor(g[:, 0:n, :], top_f[:, 0:n, k:k + 1].to_broadcast(at),
                                           iota[:, :].rearrange("p (a e) -> p a e", a=1).to_broadcast(at), ALU.is_equal))
                    link(dve.tensor_tensor(g[:, 0:n, :], g[:, 0:n, :],
                                           gw[:, 1 + k, 0:n].rearrange("p (n a) -> p n a", a=1).to_broadcast(at), ALU.mult))
                dve.tensor_tensor(gate[:, 0:n, :], gate[:, 0:n, :], gate2[:, 0:n, :], ALU.add).then_inc(S_(gate_ready), 1)
                wait(gateT_ready)
                link(dve.tensor_copy(gate_t[:, 0:w], psB[0:NE, 0:w]))
                split(gate_t[:, 0:w], NE)

                def experts(c, m, done):
                    for e in range(NE):
                        k = BC * (2 + e % 2)
                        dve.wait_ge(S_(relu_ready), done + e + 1)
                        dve.wait_ge(S_(hid_used), done + max(e - 1, 0) + 1)
                        dve.tensor_tensor(hid_g[e % 2][:, 0:m], hid[e % 2][:, 0:m], psB[:, k:k + m],
                                          ALU.mult).then_inc(S_(gated), 1)

                tile_loop(dve, blk, w, experts)
                dve.wait_ge(S_(hid_used), wait.base(NTL * NE) + NE * len(cut(w)) + 1)
                dve.tensor_tensor(res[:, 0:w], psA[0:DM, 0:w], xn[:, 0:w], ALU.add).then_inc(S_(hr_ready), 1)
                layernorm(nrm, gamma, beta, h1).then_inc(S_(out_ready), 1)
                if w == BLK:
                    assert n_link[0] == CHAIN, n_link

            blocks(dve, body)


def lay_out(x):
    f = {k: np.ascontiguousarray(v) for k, v in x.items()}
    c = f["x"].reshape(B // GI, 2, 2, H // 16, 16, W, CIN)
    c = c.transpose(0, 4, 6, 2, 3, 1, 5).reshape(B // GI, 16 * CIN, NB * P)
    sw = np.stack([f[f"L0_tok_sw{i}"] for i in range(LAYERS)])
    sw = sw.reshape(LAYERS, CH, CH, M, KG, J).transpose(0, 5, 1, 4, 3, 2).reshape(LAYERS * J, CH, KG * M, CH)
    out = {
        "coords": c, "sw": sw, "dft": dft_constants(),
        "cw": np.stack([f[f"L0_tok_cw{i}"].T for i in range(LAYERS)]),
        "cb": np.stack([f[f"L0_tok_cb{i}"] for i in range(LAYERS)]),
        "fc0_w": f["L0_tok_fc0_w"], "fc0_b": f["L0_tok_fc0_b"], "fc1_w": f["L0_tok_fc1_w"],
        "fc1_b": f["L0_tok_fc1_b"], "fc2_w": f["L0_tok_fc2_w"], "fc2_b": f["L0_tok_fc2_b"],
        "average": np.full((DM, DM), 1 / DM, np.float32),
        "center": (np.eye(DM) - 1 / DM).astype(np.float32),
        "iota": np.tile(np.arange(NE, dtype=np.float32), (P, 1)),
        "cls": f["cls_tok"].reshape(DM, 1),
        "in_w": f["L0_attn_in_w"].T, "inproj": f["L0_attn_inproj_w"].T, "xproj": f["L0_attn_xproj_w"].T,
        "dtproj": f["L0_attn_dtproj_w"].T, "outproj": f["L0_attn_outproj_w"].T, "out_w": f["L0_attn_out_w"].T,
        "dt_b": f["L0_attn_dtproj_b"],
        "gate_w": f["L0_ffn_gate_w"], "gate_b": f["L0_ffn_gate_b"],
        "w1": f["L0_ffn_w1"].transpose(1, 0, 2), "b1": f["L0_ffn_b1"].T,
        "w2": f["L0_ffn_w2"].transpose(1, 0, 2), "b2": f["L0_ffn_b2"],
        "gamma": f["L0_ffn_gamma"], "beta": f["L0_ffn_beta"],
    }
    for k in ("in_b", "ln_g", "ln_b", "conv_w", "conv_b", "A_log", "Dp", "out_b", "oln_g", "oln_b"):
        out[k] = f[f"L0_attn_{k}"]
    return {k: np.ascontiguousarray(v) for k, v in out.items()}


def declare(nc, arrays):
    return {k: nc.dram_tensor(f"in_{k}", v.shape, mybir.dt.from_np(v.dtype), kind="ExternalInput").ap()
            for k, v in arrays.items()}


def kernel(**inputs):
    import concourse.bacc as bacc
    from concourse.bass_utils import run_bass_kernel_spmd

    arrays = lay_out(inputs)
    nc = bacc.Bacc("TRN2", target_bir_lowering=False, num_devices=1)
    t = declare(nc, arrays)
    t["maps"] = nc.dram_tensor("maps", (B // GI, P, P), F32).ap()
    t["out"] = nc.dram_tensor("out", (DM, NTOK), F32, kind="ExternalOutput").ap()
    fno_program(nc, t)
    token_program(nc, t)
    r = run_bass_kernel_spmd(nc, [{f"in_{k}": v for k, v in arrays.items()}], core_ids=[0])
    o = np.asarray(r.results[0]["out"])
    y = np.empty((B, SEQ, DM), np.float32)
    y[:, :H] = o[:, :B * H].reshape(DM, B, H).transpose(1, 2, 0)
    y[:, H] = o[:, B * H:].T
    return y
```
